# Optimizing a Trainium2 kernel written in Bass

```python
import numpy as np
import jax
import jax.numpy as jnp

def _softmax(x, axis=-1):
    return jax.nn.softmax(x, axis=axis)
def _gelu(x):
    return jax.nn.gelu(x, approximate=True)
def _silu(x):
    return jax.nn.silu(x)
def _sigmoid(x):
    return jax.nn.sigmoid(x)
def _layernorm(x, axis=-1, eps=1e-5):
    m = jnp.mean(x, axis=axis, keepdims=True)
    v = jnp.var(x, axis=axis, keepdims=True)
    return (x - m) / jnp.sqrt(v + eps)
def _scatter_add(tgt, idx, src, axis=0):
    return tgt.at[idx].add(src)
def _segment_sum(src, seg, n):
    return jax.ops.segment_sum(src, seg, n)

kernel_name = 'mk_conv_preact_d4_conv_nchw16_e6315d'

def setup_inputs(seed: int = 0):
    np.random.seed(seed)
    _w = jnp.asarray
    def _rec_inputs():
        import jax
        import jax.numpy as jnp
        _gk = jax.random.key(seed)
        x = 0.03123 + 0.2782 * jax.random.normal(jax.random.fold_in(_gk, 1), (512, 16, 64, 64), jnp.float32)
        return x
    x = _rec_inputs()
    def _L0_conv_setup():
        import jax, jax.numpy as jnp
        import numpy as np
        B, C, N = (512, 16, 64)
        EPS = 1e-06

        def sparsemax(z):
            n = z.shape[-1]
            z_sorted = jnp.sort(z, axis=-1)[..., ::-1]
            cum = jnp.cumsum(z_sorted, axis=-1)
            k = jnp.arange(1, n + 1, dtype=z.dtype)
            support = 1.0 + k * z_sorted > cum
            k_z = jnp.sum(support, axis=-1, keepdims=True).astype(jnp.int32)
            cum_k = jnp.take_along_axis(cum, k_z - 1, axis=-1)
            tau = (cum_k - 1.0) / k_z.astype(z.dtype)
            return jnp.maximum(z - tau, 0.0)

        def _sym_matfunc(mat, fn):
            w, v = jnp.linalg.eigh(mat)
            return jnp.einsum('...ij,...j,...kj->...ik', v, fn(w), v)
        key = jax.random.key(seed)
        k1, k2 = jax.random.split(key)
        a = jax.random.normal(k1, (B, C, N, N), dtype=jnp.float32)
        x = jnp.einsum('bcij,bckj->bcik', a, a) / N + jnp.eye(N, dtype=jnp.float32)
        weights = jax.random.uniform(k2, (C, C), dtype=jnp.float32)
        return {'x': x, 'weights': weights}
    _L0_conv_all = _L0_conv_setup()
    _L0_conv_in = {k: v for k, v in _L0_conv_all.items() if k in ('weights', )}
    del _L0_conv_all

    def _L1_conv_setup():
        import jax, jax.numpy as jnp
        import numpy as np
        OUT_CHANNELS = 16
        IN_CHANNELS = 16
        EPS = 1e-08
        NEG_SLOPE = 0.1
        key = jax.random.key(seed)
        k1, _ = jax.random.split(key)
        x = jax.random.normal(k1, (16, IN_CHANNELS, 512, 512), dtype=jnp.float32)
        pattern = jnp.array([0, 1, 0, 0, 1, 0, 0, 1, 0, 0, 1, 0, 0, 1, 0, 0], dtype=jnp.float32)
        w = pattern - 0.01
        b = jnp.zeros((1,), dtype=jnp.float32)
        return {'x': x, 'w': w, 'b': b}
    _L1_conv_all = _L1_conv_setup()
    _L1_conv_in = {k: v for k, v in _L1_conv_all.items() if k in ('w', 'b', )}
    del _L1_conv_all

    def _L2_conv_setup():
        import jax, jax.numpy as jnp
        import numpy as np
        K_SIZE = 3
        PAD = K_SIZE // 2

        def _diag_L(n, k):
            half = k // 2
            d = np.zeros(n, dtype=np.float32)
            d[:half] = 1.0
            d[n - half:] = 1.0
            if 2 * half < k:
                d[half] = 1.0
            return d

        def _circular_pad(w, H, W, k, p):
            w = jnp.roll(jnp.pad(jnp.flip(w, -1), ((0, 0), (0, 0), (0, 0), (0, W - k))), -p, axis=-1)
            w = jnp.roll(jnp.pad(jnp.flip(w, -2), ((0, 0), (0, 0), (0, H - k), (0, 0))), -p, axis=-2)
            return w
        key = jax.random.key(seed)
        kx, kw = jax.random.split(key)
        x = jax.random.normal(kx, (16, 16, 256, 256), dtype=jnp.float32)
        weight = jax.random.normal(kw, (16, 16, 3, 3), dtype=jnp.float32) * (2.0 / (16 * 9)) ** 0.5
        return {'x': x, 'weight': weight}
    _L2_conv_all = _L2_conv_setup()
    _L2_conv_in = {k: v for k, v in _L2_conv_all.items() if k in ('weight', )}
    del _L2_conv_all

    def _L3_conv_setup():
        import jax, jax.numpy as jnp
        import numpy as np
        K_SIZE = 3
        PAD = K_SIZE // 2

        def _diag_L(n, k):
            half = k // 2
            d = np.zeros(n, dtype=np.float32)
            d[:half] = 1.0
            d[n - half:] = 1.0
            if 2 * half < k:
                d[half] = 1.0
            return d

        def _circular_pad(w, H, W, k, p):
            w = jnp.roll(jnp.pad(jnp.flip(w, -1), ((0, 0), (0, 0), (0, 0), (0, W - k))), -p, axis=-1)
            w = jnp.roll(jnp.pad(jnp.flip(w, -2), ((0, 0), (0, 0), (0, H - k), (0, 0))), -p, axis=-2)
            return w
        key = jax.random.key(seed)
        kx, kw = jax.random.split(key)
        x = jax.random.normal(kx, (16, 16, 256, 256), dtype=jnp.float32)
        weight = jax.random.normal(kw, (16, 16, 3, 3), dtype=jnp.float32) * (2.0 / (16 * 9)) ** 0.5
        return {'x': x, 'weight': weight}
    _L3_conv_all = _L3_conv_setup()
    _L3_conv_in = {k: v for k, v in _L3_conv_all.items() if k in ('weight', )}
    del _L3_conv_all

    return {
        "x": x,
        "L0_conv_weights": _L0_conv_in["weights"],
        "L1_conv_w": _L1_conv_in["w"],
        "L1_conv_b": _L1_conv_in["b"],
        "L2_conv_weight": _L2_conv_in["weight"],
        "L3_conv_weight": _L3_conv_in["weight"],
    }

def reference(x, L0_conv_weights, L1_conv_w, L1_conv_b, L2_conv_weight, L3_conv_weight):
    import jax
    import jax.numpy as jnp
    def _L0_conv_ref(x, weights):
        import jax, jax.numpy as jnp
        import numpy as np
        B, C, N = (512, 16, 64)
        EPS = 1e-06

        def sparsemax(z):
            n = z.shape[-1]
            z_sorted = jnp.sort(z, axis=-1)[..., ::-1]
            cum = jnp.cumsum(z_sorted, axis=-1)
            k = jnp.arange(1, n + 1, dtype=z.dtype)
            support = 1.0 + k * z_sorted > cum
            k_z = jnp.sum(support, axis=-1, keepdims=True).astype(jnp.int32)
            cum_k = jnp.take_along_axis(cum, k_z - 1, axis=-1)
            tau = (cum_k - 1.0) / k_z.astype(z.dtype)
            return jnp.maximum(z - tau, 0.0)

        def _sym_matfunc(mat, fn):
            w, v = jnp.linalg.eigh(mat)
            return jnp.einsum('...ij,...j,...kj->...ik', v, fn(w), v)
        w_sm = sparsemax(weights)
        logs = _sym_matfunc(x, lambda w: jnp.log(jnp.maximum(w, EPS)))
        mixed = jnp.einsum('ic,bcmn->bimn', w_sm, logs)
        return _sym_matfunc(mixed, jnp.exp)

    def _L1_conv_ref(x, w, b):
        import jax, jax.numpy as jnp
        import numpy as np
        OUT_CHANNELS = 16
        IN_CHANNELS = 16
        EPS = 1e-08
        NEG_SLOPE = 0.1
        W2 = jnp.stack([jnp.roll(w, o) for o in range(OUT_CHANNELS)])
        y = jnp.einsum('bchw,oc->bohw', x, W2) + b[0]
        y = jnp.where(y >= 0, y, NEG_SLOPE * y)
        mn = jnp.min(y, axis=(2, 3), keepdims=True)
        mx = jnp.max(y, axis=(2, 3), keepdims=True)
        return (y - mn) / (mx - mn + EPS)

    def _L2_conv_ref(x, weight):
        import jax, jax.numpy as jnp
        import numpy as np
        K_SIZE = 3
        PAD = K_SIZE // 2

        def _diag_L(n, k):
            half = k // 2
            d = np.zeros(n, dtype=np.float32)
            d[:half] = 1.0
            d[n - half:] = 1.0
            if 2 * half < k:
                d[half] = 1.0
            return d

        def _circular_pad(w, H, W, k, p):
            w = jnp.roll(jnp.pad(jnp.flip(w, -1), ((0, 0), (0, 0), (0, 0), (0, W - k))), -p, axis=-1)
            w = jnp.roll(jnp.pad(jnp.flip(w, -2), ((0, 0), (0, 0), (0, H - k), (0, 0))), -p, axis=-2)
            return w
        B, Ci, H, W = x.shape
        k, p = (K_SIZE, PAD)
        w_pad = _circular_pad(weight, H, W, k, p)
        dL = jnp.asarray(np.outer(_diag_L(H, k), _diag_L(W, k)))
        Lw = jnp.fft.fft2(w_pad * dL)
        Kx = jnp.fft.ifft2(x, norm='ortho')
        z = jnp.einsum('oihw,bihw->bohw', Lw, Kx)
        y = jnp.fft.fft2(z, norm='ortho')
        return jnp.real(y).astype(x.dtype)

    def _L3_conv_ref(x, weight):
        import jax, jax.numpy as jnp
        import numpy as np
        K_SIZE = 3
        PAD = K_SIZE // 2

        def _diag_L(n, k):
            half = k // 2
            d = np.zeros(n, dtype=np.float32)
            d[:half] = 1.0
            d[n - half:] = 1.0
            if 2 * half < k:
                d[half] = 1.0
            return d

        def _circular_pad(w, H, W, k, p):
            w = jnp.roll(jnp.pad(jnp.flip(w, -1), ((0, 0), (0, 0), (0, 0), (0, W - k))), -p, axis=-1)
            w = jnp.roll(jnp.pad(jnp.flip(w, -2), ((0, 0), (0, 0), (0, H - k), (0, 0))), -p, axis=-2)
            return w
        B, Ci, H, W = x.shape
        k, p = (K_SIZE, PAD)
        w_pad = _circular_pad(weight, H, W, k, p)
        dL = jnp.asarray(np.outer(_diag_L(H, k), _diag_L(W, k)))
        Lw = jnp.fft.fft2(w_pad * dL)
        Kx = jnp.fft.ifft2(x, norm='ortho')
        z = jnp.einsum('oihw,bihw->bohw', Lw, Kx)
        y = jnp.fft.fft2(z, norm='ortho')
        return jnp.real(y).astype(x.dtype)

    def _gn(v, G=8, eps=1e-5):
        B_, C_, H_, W_ = v.shape
        g = v.reshape(B_, G, C_ // G, H_, W_)
        m = jnp.mean(g, axis=(2, 3, 4), keepdims=True)
        s = jnp.var(g, axis=(2, 3, 4), keepdims=True)
        return ((g - m) / jnp.sqrt(s + eps)).reshape(v.shape)

    def _ln_c(v, eps=1e-6):
        m = jnp.mean(v, axis=1, keepdims=True)
        s = jnp.var(v, axis=1, keepdims=True)
        return (v - m) / jnp.sqrt(s + eps)

    def _ln_t(v, eps=1e-5):
        m = jnp.mean(v, axis=-1, keepdims=True)
        s = jnp.var(v, axis=-1, keepdims=True)
        return (v - m) / jnp.sqrt(s + eps)

    def _to_tokens(v):
        B_, C_, H_, W_ = v.shape
        return v.reshape(B_, C_, H_ * W_).transpose(0, 2, 1)
    def _from_tokens(t, like):
        B_, C_, H_, W_ = like.shape
        return t.transpose(0, 2, 1).reshape(B_, C_, H_, W_)

    x = x + _L0_conv_ref(_gn(x), L0_conv_weights)
    x = x + _L1_conv_ref(_gn(x), L1_conv_w, L1_conv_b)
    x = x + _L2_conv_ref(_gn(x), L2_conv_weight)
    x = x + _L3_conv_ref(_gn(x), L3_conv_weight)
    return x


_drawn_inputs = setup_inputs


def setup_inputs(seed=0):
    import zlib

    import numpy as np

    out = dict(_drawn_inputs(seed))
    spreads = {}
    factors = {}
    for name, (base, spread) in spreads.items():
        noise = np.random.default_rng([zlib.crc32(name.encode()), seed]).standard_normal(out[name].shape)
        drawn = base * np.exp(spread * noise) if base else spread * noise
        out[name] = jnp.asarray(drawn.astype(out[name].dtype))
    for name, factor in factors.items():
        out[name] = (out[name] * factor).astype(out[name].dtype)
    return out
```

```python
import math
from contextlib import ExitStack

import concourse.bass as bass
from concourse import mybir

F32 = mybir.dt.float32
ALU = mybir.AluOpType
ACT = mybir.ActivationFunctionType
AX = mybir.AxisListType

P = 128
N = 64
C = 16
HALF = P // 2
CG = C // 2
LOT = 2
W = LOT * CG * N
LOTS = 2
BANK = 512
TAPS = 3
PADN = N + 2
BB = P // C
ROWS = BANK // N
CHUNKS = N // ROWS
GN_EPS = 1e-5
MINMAX_EPS = 1e-8
SLOPE = 0.1
LOG_FLOOR = 1e-6


class Plan:
    RADIUS = 90.51
    LOG_STEPS = (
        (2.48664179425, -3.03870824678, 1.00220376711, 1.07155469039, 0.632705325253),
        (2.61933212627, -3.80283943677, 1.48950710891, 1.2922347781, 0.90383002991),
        (2.69067040556, -4.11712810476, 1.70112033155, 1.36504105955, 0.999427786258),
        (2.56604567804, -3.9069764105, 1.60870413922, 1.36308823059, 0.97877302381),
        (2.60430779298, -4.05129193845, 1.71159622702, 1.40615600542, 0.994119439656),
        (2.59484189219, -4.19626471277, 1.84293181717, 1.46194803445, 1.0680300449),
        (2.69712393638, -3.93652344719, 1.58809939822, 1.36343258865, 0.779469169479),
        (2.64018609512, -3.83349735037, 1.50761813188, 1.3005398153, 0.872685135399),
        (2.77681465619, -3.8723337268, 1.47967451394, 1.28410260361, 0.749055549574),
        (2.7681637885, -4.40451815161, 1.8569101296, 1.33268451869, 1.24371376752),
        (2.9949428489, -4.13413563993, 1.66268152647, 1.38252628239, 0.494085541651),
        (2.97249388786, -4.13964947462, 1.50762386785, 1.06483761741, 1.09979172194),
        (3.08317941948, -3.76209818287, 1.29735697322, 1.27677717961, 0.371472152037),
        (3.19523579499, -2.99897215643, 1.08673732843, 1.44195707469, -0.449954591229),
        (2.48218988423, -1.77128186707, 0.453908311571, 1.08389585929, -0.278591503352),
        (1.83558929048, -1.17219026936, 0.336605805469, 3.24293805576, -1.37157998663),
    )
    LOG_CONST = -12.4423939591
    EXP_SQUARINGS = 3
    EXP_MIDDLE = (math.log(LOG_FLOOR) + math.log(RADIUS)) / 2 / 2 ** EXP_SQUARINGS
    EXP_POLY = (0.00489026101281, 0.0210741285655, 0.0738744979625, 0.866975325236, 0.120046341077,
                2.97006843862, 0.500000819739, 0.999999837917, 0.999999968679)


def build(nc, x, w_mix, w_ring, bias_ring, w_conv2, w_conv3, out):
    B = x.shape[0]
    logs = nc.dram_tensor("logs", (B, C, N, N), F32).ap()
    mixed = nc.dram_tensor("mixed", (B, C, N, N), F32).ap()
    x1 = nc.dram_tensor("x1", (B, C, N, N), F32).ap()
    spectral_log(nc, x, logs)
    mix_channels(nc, logs, w_mix, mixed)
    spectral_exp(nc, mixed, x, x1)
    conv_layers(nc, x1, w_ring, bias_ring, w_conv2, w_conv3, out)


def lot_view(t):
    return t.rearrange("b (g c) h w -> b (c h) g w", c=2)


def lot_product(pe, psum, lhsT, rhs):
    pe.nop(nofuse=True)
    for window in range(LOT):
        for j in range(CG):
            for half in range(2):
                b = (window + half) % LOT
                rows = slice(half * HALF, half * HALF + HALF)
                cols = slice(b * BANK + j * N, b * BANK + j * N + N)
                last = pe.matmul(psum[rows, cols], lhsT[rows, cols], rhs[rows, cols], start=True, stop=True)
    return last


def spectral_log(nc, x, logs):
    B = x.shape[0]
    GROUPS = B // (LOT * LOTS)
    STEPS = len(Plan.LOG_STEPS)
    COUNT = 2 * N * N
    LOG_EPS = math.log(LOG_FLOOR)
    x_v, logs_v = lot_view(x), lot_view(logs)

    rows, scale = [], 1.0
    for a, b, c, p, q in Plan.LOG_STEPS:
        s2 = scale * scale
        rows.append((0.5 * p * s2, c / b * s2, 0.5 * q * s2 * s2, b / a * s2))
        scale *= a
    SIGN_SCALE = scale
    L_START = 0.5 * (Plan.LOG_CONST - LOG_EPS)

    with ExitStack() as ctx:
        def sb(name, shape):
            return ctx.enter_context(nc.sbuf_tensor(name, shape, F32))

        def sem(name):
            return ctx.enter_context(nc.semaphore(name))

        def sems(name, n=LOTS):
            return [sem(f"{name}{i}") for i in range(n)]

        ident = sb("log_ident", [P, W])
        minus_mean = sb("log_minus_mean", [P, P])
        table = sb("log_table", [P, 4 * STEPS])
        root_bias = sb("log_root_bias", [P, 1])
        xin = sb("log_xin", [P, LOTS, W])
        xc = sb("log_xc", [P, LOTS, W])
        F = sb("log_F", [P, LOTS, W])
        X = sb("log_X", [P, LOTS, W])
        XT = sb("log_XT", [P, LOTS, W])
        Y = sb("log_Y", [P, LOTS, W])
        Q = sb("log_Q", [P, LOTS, W])
        L = sb("log_L", [P, LOTS, W])
        credit = sb("log_credit", [P, LOTS])
        stat = sb("log_stat", [P, LOTS, 4, LOT * CG])
        ps = [[ctx.enter_context(nc.psum_tensor(f"log_ps{i}{j}", [P, W], F32)) for j in range(2)]
              for i in range(LOTS)]

        consts = sem("log_consts")
        const_step = sem("log_const_step")
        loaded = sems("log_loaded", LOTS)
        sums_ready = sems("log_sums")
        mean_ready = sems("log_mean")
        mean_copied = sems("log_mean_copied")
        xc_ready = sems("log_xc_ready")
        squares_ready = sems("log_squares")
        sqsums_ready = sems("log_sqsums")
        xct_ready = sems("log_xct")
        var_ready = sems("log_var")
        root_ready = sems("log_root")
        scale_ready = sems("log_scale")
        sym_ready = sems("log_sym")
        l_started = sems("log_l_started")
        x_ready = sems("log_x_ready")
        blocks_turned = sems("log_blocks_turned")
        xt_ready = sems("log_xt_ready")
        l1_done = sems("log_l1_done")
        l2_done = sems("log_l2_done")
        y_ready = sems("log_y_ready")
        y_copied = sems("log_y_copied")
        y2_ready = sems("log_y2_ready")
        q_ready = sems("log_q_ready")
        u_ready = sems("log_u_ready")
        v_ready = sems("log_v_ready")
        f0_ready = sems("log_f0_ready")
        f_ready = sems("log_f_ready")
        stored = sems("log_stored")
        block = ctx.enter_context(nc.Block())

        CONSTS = 4

        def grouped(t, l):
            return t[:, l, :].rearrange("p (m n) -> p m n", n=N)

        def spread(t):
            return t.unsqueeze(2).to_broadcast([P, LOT * CG, N])

        @block.gpsimd
        def _(pool):
            build_identity(pool, ident, const_step, consts)
            pool.memset(minus_mean[:, :], -1.0 / COUNT).then_inc(consts, 1)
            pool.memset(root_bias[:, :], GN_EPS * (2.0 * Plan.RADIUS) ** 2).then_inc(consts, 1)
            for l in range(LOTS):
                pool.memset(credit[:, l:l + 1], 0.0).then_inc(stored[l], 1)
            for k, row in enumerate(rows):
                for i, value in enumerate(row):
                    last = pool.memset(table[:, 4 * k + i:4 * k + i + 1], float(value))
            last.then_inc(consts, 1)

        @block.sync
        def _(sp):
            def load(first):
                for l in range(LOTS):
                    for b in range(LOT):
                        sp.dma_start(xin[:, l, b * BANK:(b + 1) * BANK].rearrange("p (g n) -> p g n", n=N),
                                     x_v[first + l * LOT + b]).then_inc(loaded[l], 16)

            def store(g):
                for l in range(LOTS):
                    sp.wait_ge(f_ready[l], g + 1)
                    for b in range(LOT):
                        sp.dma_start(logs_v[g * (LOT * LOTS) + l * LOT + b],
                                     F[:, l, b * BANK:(b + 1) * BANK].rearrange("p (g n) -> p g n", n=N)
                                     ).then_inc(stored[l], 16)

            def reload(g):
                for l in range(LOTS):
                    sp.wait_ge(xc_ready[l], g)
                load(g * (LOT * LOTS))

            load(0)
            reload(1)
            with sp.Fori(0, GROUPS - 2) as g:
                reload(g + 2)
                store(g)
            store(GROUPS - 2)
            store(GROUPS - 1)
            for l in range(LOTS):
                sp.wait_ge(stored[l], 16 * LOT * GROUPS + 1)


        @block.tensor
        def _(pe):
            pe.wait_ge(consts, CONSTS)

            def mean(g):
                for l in range(LOTS):
                    pe.wait_ge(sums_ready[l], g + 1)
                    pe.matmul(ps[l][1][:, 0:LOT * CG], minus_mean[:, :], stat[:, l, 0, :],
                              start=True, stop=True).then_inc(mean_ready[l], 1)

            def transposed(g):
                for l in range(LOTS):
                    pe.wait_ge(xc_ready[l], g + 1)
                    lot_product(pe, ps[l][1], xc[:, l], ident[:, :]).then_inc(xct_ready[l], 1)

            def variance(g):
                for l in range(LOTS):
                    pe.wait_ge(sqsums_ready[l], g + 1)
                    pe.matmul(ps[l][0][:, 0:LOT * CG], minus_mean[:, :], stat[:, l, 1, :],
                              start=True, stop=True).then_inc(var_ready[l], 1)

            def steps(g):
                with pe.Fori(0, STEPS) as k:
                    for l in range(LOTS):
                        pe.wait_ge(x_ready[l], g * (STEPS + 1) + k + 1)
                        lot_product(pe, ps[l][0], X[:, l], X[:, l]).then_inc(y_ready[l], 1)
                    for l in range(LOTS):
                        pe.wait_ge(y_copied[l], g * STEPS + k + 1)
                        lot_product(pe, ps[l][1], Y[:, l], Y[:, l]).then_inc(y2_ready[l], 1)
                    for l in range(LOTS):
                        pe.wait_ge(xt_ready[l], g * STEPS + k + 1)
                        pe.wait_ge(q_ready[l], g * STEPS + k + 1)
                        lot_product(pe, ps[l][0], XT[:, l], Q[:, l]).then_inc(u_ready[l], 1)

            def signed_log(g, l):
                pe.wait_ge(x_ready[l], g * (STEPS + 1) + STEPS + 1)
                pe.wait_ge(l2_done[l], g * STEPS + STEPS)
                lot_product(pe, ps[l][0], X[:, l], L[:, l]).then_inc(v_ready[l], 1)

            mean(0)
            transposed(0)
            variance(0)
            with pe.Fori(0, GROUPS - 1) as g:
                steps(g)
                signed_log(g, 0)
                mean(g + 1)
                signed_log(g, 1)
                transposed(g + 1)
                variance(g + 1)
            steps(GROUPS - 1)
            for l in range(LOTS):
                signed_log(GROUPS - 1, l)

        @block.scalar
        def _(act):
            act.wait_ge(consts, CONSTS)

            def prepare(g, after_group):
                for l in range(LOTS):
                    act.wait_ge(mean_ready[l], g + 1)
                    nc.scalar.copy(stat[:, l, 2, :], ps[l][1][:, 0:LOT * CG]).then_inc(mean_copied[l], 1)
                for l in range(LOTS):
                    act.wait_ge(xc_ready[l], g + 1)
                    nc.scalar.square(Y[:, l, :], xc[:, l, :]).then_inc(squares_ready[l], 1)
                for l in range(LOTS):
                    if after_group:
                        act.wait_ge(f0_ready[l], g)
                    nc.scalar.mul(L[:, l, :], ident[:, :], L_START).then_inc(l_started[l], 1)
                    act.wait_ge(var_ready[l], g + 1)
                    nc.scalar.activation(stat[:, l, 3, :], ps[l][0][:, 0:LOT * CG], ACT.Sqrt, bias=root_bias[:, 0:1],
                                         scale=-(2.0 * Plan.RADIUS) ** 2).then_inc(root_ready[l], 1)

            def steps(g):
                with act.Fori(0, STEPS) as k:
                    for l in range(LOTS):
                        act.wait_ge(y_ready[l], g * STEPS + k + 1)
                        nc.scalar.copy(Y[:, l, :], ps[l][0][:, :]).then_inc(y_copied[l], 1)

            prepare(0, False)
            with act.Fori(0, GROUPS - 1) as g:
                steps(g)
                prepare(g + 1, True)
            steps(GROUPS - 1)

        @block.vector
        def _(dve):
            dve.wait_ge(consts, CONSTS)

            def row_sums(g, l):
                dve.wait_ge(loaded[l], 16 * LOT * g + 16 * LOT)
                nc.vector.tensor_reduce(stat[:, l, 0, :], grouped(xin, l), AX.X, ALU.add).then_inc(sums_ready[l], 1)

            def centre(g, l):
                dve.wait_ge(mean_copied[l], g + 1)
                nc.vector.tensor_tensor(grouped(xc, l), grouped(xin, l), spread(stat[:, l, 2, :]),
                                        ALU.add).then_inc(xc_ready[l], 1)

            def square_sums(g, l):
                dve.wait_ge(squares_ready[l], g + 1)
                nc.vector.tensor_reduce(stat[:, l, 1, :], grouped(Y, l), AX.X, ALU.add).then_inc(sqsums_ready[l], 1)

            def start(g, l):
                dve.wait_ge(xct_ready[l], g + 1)
                nc.vector.tensor_tensor(Q[:, l, :], xc[:, l, :], ps[l][1][:, :], ALU.add).then_inc(sym_ready[l], 1)
                dve.wait_ge(root_ready[l], g + 1)
                nc.vector.reciprocal(stat[:, l, 3, :], stat[:, l, 3, :]).then_inc(scale_ready[l], 1)
                dve.wait_ge(scale_ready[l], g + 1)
                dve.wait_ge(sym_ready[l], g + 1)
                nc.vector.tensor_tensor(grouped(X, l), grouped(Q, l), spread(stat[:, l, 3, :]),
                                        ALU.mult).then_inc(x_ready[l], 1)

            def steps(g):
                with dve.Fori(0, STEPS) as k:
                    for l in range(LOTS):
                        dve.wait_ge(x_ready[l], g * (STEPS + 1) + k + 1)
                        nc.vector.transpose(XT[:, l], X[:, l]).then_inc(blocks_turned[l], 1)
                    for l in range(LOTS):
                        dve.wait_ge(blocks_turned[l], g * STEPS + k + 1)
                        swap_blocks(nc, XT[:, l], X[:, l]).then_inc(xt_ready[l], 1)
                        dve.wait_ge(y_copied[l], g * STEPS + k + 1)
                        dve.wait_ge(l_started[l], g + 1)
                        nc.vector.scalar_tensor_tensor(L[:, l, :], Y[:, l, :], table[:, bass.ds(4 * k, 1)],
                                                       L[:, l, :], ALU.mult, ALU.add).then_inc(l1_done[l], 1)
                    for l in range(LOTS):
                        dve.wait_ge(y2_ready[l], g * STEPS + k + 1)
                        nc.vector.scalar_tensor_tensor(Q[:, l, :], ps[l][1][:, :], table[:, bass.ds(4 * k + 1, 1)],
                                                       Y[:, l, :], ALU.mult, ALU.add).then_inc(q_ready[l], 1)
                        dve.wait_ge(l1_done[l], g * STEPS + k + 1)
                        nc.vector.scalar_tensor_tensor(L[:, l, :], ps[l][1][:, :], table[:, bass.ds(4 * k + 2, 1)],
                                                       L[:, l, :], ALU.mult, ALU.add).then_inc(l2_done[l], 1)
                    for l in range(LOTS):
                        dve.wait_ge(u_ready[l], g * STEPS + k + 1)
                        nc.vector.scalar_tensor_tensor(X[:, l, :], ps[l][0][:, :], table[:, bass.ds(4 * k + 3, 1)],
                                                       X[:, l, :], ALU.mult, ALU.add).then_inc(x_ready[l], 1)

            def finish(g, l):
                dve.wait_ge(v_ready[l], g + 1)
                dve.wait_ge(l2_done[l], g * STEPS + STEPS)
                nc.vector.scalar_tensor_tensor(Q[:, l, :], ps[l][0][:, :], SIGN_SCALE, L[:, l, :],
                                               ALU.mult, ALU.add).then_inc(f0_ready[l], 1)
                dve.wait_ge(f0_ready[l], g + 1)
                dve.wait_ge(stored[l], 16 * LOT * g + 1)
                nc.vector.scalar_tensor_tensor(F[:, l, :], ident[:, :], LOG_EPS, Q[:, l, :],
                                               ALU.mult, ALU.add).then_inc(f_ready[l], 1)

            for part in (row_sums, centre, square_sums, start):
                for l in range(LOTS):
                    part(0, l)
            with dve.Fori(0, GROUPS - 1) as g:
                steps(g)
                for l in range(LOTS):
                    row_sums(g + 1, l)
                for l in range(LOTS):
                    centre(g + 1, l)
                for l in range(LOTS):
                    finish(g, l)
                    square_sums(g + 1, l)
                for l in range(LOTS):
                    start(g + 1, l)
            steps(GROUPS - 1)
            for l in range(LOTS):
                finish(GROUPS - 1, l)


def swap_blocks(nc, dst, src):
    for q in range(P // 32):
        there = q ^ 1
        s = src[32 * q:32 * q + 32, :].rearrange("p (m k n) -> p m k n", k=2, n=32)[:, :, 1 - q % 2, :]
        d = dst[32 * there:32 * there + 32, :].rearrange("p (m k n) -> p m k n", k=2, n=32)[:, :, q % 2, :]
        last = nc.vector.transpose(d, s)
    return last


def build_identity(pool, ident, step, done):
    v = ident[:, :].rearrange("p (m n) -> p m n", n=N)
    pool.memset(ident[:, :], 0.0).then_inc(step, 1)
    pool.wait_ge(step, 1)
    pool.affine_select(out=v, in_=v, compare_op=ALU.not_equal, fill=1.0, base=0,
                       pattern=[[0, ident.shape[1] // N], [-1, N]], channel_multiplier=1).then_inc(step, 1)
    pool.wait_ge(step, 2)
    pool.affine_select(out=v, in_=v, compare_op=ALU.not_equal, fill=1.0, base=-HALF,
                       pattern=[[0, ident.shape[1] // N], [-1, N]], channel_multiplier=1).then_inc(done, 1)


def mix_channels(nc, logs, w_rows, mixed):
    B = logs.shape[0]
    TILES = B // BB
    BUFS = 2
    PIX = N * N
    logs_v = logs.rearrange("(t b) c h w -> t (b c) (h w)", b=BB)
    mixed_v = mixed.rearrange("(t b) c h w -> t (b c) (h w)", b=BB)

    with ExitStack() as ctx:
        def sb(name, shape):
            return ctx.enter_context(nc.sbuf_tensor(name, shape, F32))

        def sem(name):
            return ctx.enter_context(nc.semaphore(name))

        z = sb("mix_z", [P, C])
        above = sb("mix_above", [P, C, C])
        part = sb("mix_part", [P, C, C])
        count = sb("mix_count", [P, C])
        total = sb("mix_total", [P, C])
        support = sb("mix_support", [P, C])
        held = sb("mix_held", [P, C])
        col = sb("mix_col", [P, 4])
        sparse = sb("mix_sparse", [P, C])
        mask = sb("mix_mask", [P, P])
        spread = sb("mix_spread", [P, P])
        eye = sb("mix_eye", [P, P])
        lhsT = sb("mix_lhsT", [P, P])
        credit = sb("mix_credit", [P, BUFS + 1])
        src = sb("mix_src", [P, BUFS, PIX])
        dst = sb("mix_dst", [P, BUFS, PIX])
        ps = ctx.enter_context(nc.psum_tensor("mix_ps", [P, 8, BANK], F32))

        z_loaded = sem("mix_z_loaded")
        mask_step = sem("mix_mask_step")
        consts = sem("mix_consts")
        chain = sem("mix_chain")
        loaded = [sem(f"mix_loaded{i}") for i in range(BUFS)]
        stored = [sem(f"mix_stored{i}") for i in range(BUFS)]
        half_ready = [sem(f"mix_half_ready{i}") for i in range(2)]
        half_copied = [sem(f"mix_half_copied{i}") for i in range(2)]
        block = ctx.enter_context(nc.Block())

        @block.gpsimd
        def _(pool):
            build_block_mask(pool, mask, mask_step, consts)
            pool.memset(eye[:, :], 0.0).then_inc(mask_step, 1)
            pool.wait_ge(mask_step, 3)
            pool.affine_select(out=eye[:, :], in_=eye[:, :], compare_op=ALU.not_equal, fill=1.0, base=0,
                               pattern=[[-1, P]], channel_multiplier=1).then_inc(consts, 1)
            for i in range(BUFS):
                pool.memset(credit[:, i:i + 1], 0.0).then_inc(stored[i], 1)
            pool.memset(credit[:, BUFS:BUFS + 1], 0.0).then_inc(half_copied[1], 1)

        @block.sync
        def _(sp):
            sp.dma_start(z[:, :], w_rows).then_inc(z_loaded, 16)
            for i in range(BUFS):
                sp.dma_start(src[:, i, :], logs_v[i]).then_inc(loaded[i], 16)
            with sp.Fori(0, TILES // BUFS - 1) as t:
                for i in range(BUFS):
                    for h in range(2):
                        sp.wait_ge(half_copied[h], t * BUFS + i + 2)
                    sp.dma_start(mixed_v[t * BUFS + i], dst[:, i, :]).then_inc(stored[i], 16)
                    sp.dma_start(src[:, i, :], logs_v[t * BUFS + BUFS + i]).then_inc(loaded[i], 16)
            for i in range(BUFS):
                for h in range(2):
                    sp.wait_ge(half_copied[h], TILES - BUFS + i + 2)
                sp.dma_start(mixed_v[TILES - BUFS + i], dst[:, i, :]).then_inc(stored[i], 16)
            for i in range(BUFS):
                sp.wait_ge(stored[i], 16 * (TILES // BUFS) + 1)

        @block.vector
        def _(dve):
            done = [0]

            def link(ins):
                done[0] += 1
                ins.then_inc(chain, 1)
                dve.wait_ge(chain, done[0])

            zl = z[:, :].unsqueeze(1).to_broadcast([P, C, C])
            zj = z[:, :].unsqueeze(2).to_broadcast([P, C, C])
            dve.wait_ge(z_loaded, 16)
            link(nc.vector.tensor_tensor(above[:, :, :], zl, zj, ALU.is_ge))
            link(nc.vector.tensor_reduce(count[:, :], above[:, :, :], AX.X, ALU.add))
            link(nc.vector.tensor_tensor(part[:, :, :], above[:, :, :], zl, ALU.mult))
            link(nc.vector.tensor_reduce(total[:, :], part[:, :, :], AX.X, ALU.add))
            link(nc.vector.tensor_tensor(held[:, :], count[:, :], z[:, :], ALU.mult))
            link(nc.vector.tensor_scalar(held[:, :], held[:, :], 1.0, None, ALU.add))
            link(nc.vector.tensor_tensor(support[:, :], held[:, :], total[:, :], ALU.is_gt))
            link(nc.vector.tensor_reduce(col[:, 0:1], support[:, :], AX.X, ALU.add))
            link(nc.vector.tensor_tensor(held[:, :], support[:, :], z[:, :], ALU.mult))
            link(nc.vector.tensor_reduce(col[:, 1:2], held[:, :], AX.X, ALU.add))
            link(nc.vector.tensor_scalar(col[:, 1:2], col[:, 1:2], -1.0, None, ALU.add))
            link(nc.vector.reciprocal(col[:, 2:3], col[:, 0:1]))
            link(nc.vector.tensor_tensor(col[:, 3:4], col[:, 1:2], col[:, 2:3], ALU.mult))
            link(nc.vector.tensor_scalar(sparse[:, :], z[:, :], col[:, 3:4], 0.0, ALU.subtract, ALU.max))
            dve.wait_ge(consts, 2)
            link(nc.vector.tensor_tensor(spread[:, :].rearrange("p (b c) -> p b c", c=C),
                                         mask[:, :].rearrange("p (b c) -> p b c", c=C),
                                         sparse[:, :].unsqueeze(1).to_broadcast([P, BB, C]), ALU.mult))
            dve.wait_ge(half_ready[0], 1)
            nc.vector.tensor_copy(lhsT[:, :], ps[:, 0, 0:P]).then_inc(half_copied[0], 1)
            with dve.Fori(0, TILES // BUFS) as t:
                for i in range(BUFS):
                    dve.wait_ge(stored[i], 16 * t + 1)
                    dve.wait_ge(half_ready[0], t * BUFS + i + 2)
                    nc.vector.tensor_copy(dst[:, i, 0:PIX // 2], ps[:, 0:4, :].rearrange("p k n -> p (k n)")
                                          ).then_inc(half_copied[0], 1)

        @block.scalar
        def _(act):
            with act.Fori(0, TILES // BUFS) as t:
                for i in range(BUFS):
                    act.wait_ge(stored[i], 16 * t + 1)
                    act.wait_ge(half_ready[1], t * BUFS + i + 1)
                    nc.scalar.copy(dst[:, i, PIX // 2:PIX], ps[:, 4:8, :].rearrange("p k n -> p (k n)")
                                   ).then_inc(half_copied[1], 1)

        @block.tensor
        def _(pe):
            pe.wait_ge(consts, 2)
            pe.wait_ge(chain, 15)
            pe.matmul(ps[:, 0, 0:P], spread[:, :], eye[:, :], start=True, stop=True).then_inc(half_ready[0], 1)
            with pe.Fori(0, TILES // BUFS) as t:
                for i in range(BUFS):
                    pe.wait_ge(loaded[i], 16 * t + 16)
                    for h in range(2):
                        pe.wait_ge(half_copied[h], t * BUFS + i + 1)
                        for k in range(4 * h, 4 * h + 4):
                            last = pe.matmul(ps[:, k, :], lhsT[:, :], src[:, i, k * BANK:(k + 1) * BANK],
                                             start=True, stop=True)
                        last.then_inc(half_ready[h], 1)


def build_block_mask(pool, mask, step, done):
    v = mask[:, :].rearrange("p (b c) -> p b c", c=C)
    pool.memset(mask[:, :], 1.0).then_inc(step, 1)
    pool.wait_ge(step, 1)
    pool.affine_select(out=v, in_=v, compare_op=ALU.is_ge, fill=0.0, base=0,
                       pattern=[[-C, BB], [0, C]], channel_multiplier=1).then_inc(step, 1)
    pool.wait_ge(step, 2)
    pool.affine_select(out=v, in_=v, compare_op=ALU.is_ge, fill=0.0, base=C - 1,
                       pattern=[[C, BB], [0, C]], channel_multiplier=-1).then_inc(done, 1)


def spectral_exp(nc, mixed, x, x1):
    B = x.shape[0]
    GROUPS = B // (LOT * LOTS)
    SQUARINGS = Plan.EXP_SQUARINGS
    MIDDLE = math.exp(Plan.EXP_MIDDLE)
    z2, z1, u2, u1, v2, *w = Plan.EXP_POLY
    w0, w2, w1, w_ = (MIDDLE * c for c in w)
    mixed_v, x_v, x1_v = lot_view(mixed), lot_view(x), lot_view(x1)

    with ExitStack() as ctx:
        def sb(name, shape):
            return ctx.enter_context(nc.sbuf_tensor(name, shape, F32))

        def sem(name):
            return ctx.enter_context(nc.semaphore(name))

        def sems(name, n=LOTS):
            return [sem(f"{name}{i}") for i in range(n)]

        ident = sb("exp_ident", [P, W])
        shift = sb("exp_shift", [P, W])
        last_term = sb("exp_last_term", [P, W])
        M = sb("exp_M", [P, LOTS, W])
        XR = sb("exp_XR", [P, LOTS, W])
        S1 = sb("exp_S1", [P, LOTS, W])
        S2 = sb("exp_S2", [P, LOTS, W])
        ZT = sb("exp_Z", [P, LOTS, W])
        H1 = sb("exp_H1", [P, LOTS, W])
        H2 = sb("exp_H2", [P, LOTS, W])
        LO = sb("exp_LO", [P, LOTS, W])
        credit = sb("exp_credit", [P, LOTS])
        OUT = sb("exp_OUT", [P, LOTS, W])
        ps = [[ctx.enter_context(nc.psum_tensor(f"exp_ps{i}{j}", [P, W], F32)) for j in range(2)]
              for i in range(LOTS)]

        const_step = sem("exp_const_step")
        ident_ready = sem("exp_ident_ready")
        consts = sem("exp_consts")
        m_loaded = sems("exp_m_loaded")
        x_loaded = sems("exp_x_loaded")
        n_ready = sems("exp_n_ready")
        product_ready = sems("exp_product")
        taken = sems("exp_taken")
        g_ready = sems("exp_g_ready")
        h_step = sems("exp_h_step")
        h_ready = sems("exp_h_ready")
        lo_done = sems("exp_lo")
        e_ready = sems("exp_e_ready")
        out_ready = sems("exp_out_ready")
        stored = sems("exp_stored")
        block = ctx.enter_context(nc.Block())
        PRODUCTS = 3 + SQUARINGS
        TAKEN = 2 + SQUARINGS - 1

        @block.gpsimd
        def _(pool):
            build_identity(pool, ident, const_step, ident_ready)
            pool.wait_ge(ident_ready, 1)
            pool.tensor_scalar(shift[:, :], ident[:, :], -Plan.EXP_MIDDLE, None, ALU.mult).then_inc(consts, 1)
            pool.tensor_scalar(last_term[:, :], ident[:, :], w_, None, ALU.mult).then_inc(consts, 1)
            for l in range(LOTS):
                pool.memset(credit[:, l:l + 1], 0.0).then_inc(stored[l], 1)

        @block.sync
        def _(sp):
            def tile(t, l, b):
                return t[:, l, b * BANK:(b + 1) * BANK].rearrange("p (g n) -> p g n", n=N)

            def load(v, t, sem, first, l):
                for b in range(LOT):
                    sp.dma_start(tile(t, l, b), v[first + l * LOT + b]).then_inc(sem[l], 16)

            def store(first):
                for l in range(LOTS):
                    for b in range(LOT):
                        sp.dma_start(x1_v[first + l * LOT + b], tile(OUT, l, b)).then_inc(stored[l], 16)

            for l in range(LOTS):
                load(mixed_v, M, m_loaded, 0, l)
            for l in range(LOTS):
                load(x_v, XR, x_loaded, 0, l)
            with sp.Fori(0, GROUPS - 1) as g:
                for l in range(LOTS):
                    sp.wait_ge(n_ready[l], g + 1)
                    load(mixed_v, M, m_loaded, (g + 1) * (LOT * LOTS), l)
                for l in range(LOTS):
                    sp.wait_ge(out_ready[l], g + 1)
                    load(x_v, XR, x_loaded, (g + 1) * (LOT * LOTS), l)
                store(g * (LOT * LOTS))
            for l in range(LOTS):
                sp.wait_ge(out_ready[l], GROUPS)
            store((GROUPS - 1) * (LOT * LOTS))
            for l in range(LOTS):
                sp.wait_ge(stored[l], 16 * LOT * GROUPS + 1)

        @block.tensor
        def _(pe):
            with pe.Fori(0, GROUPS) as g:
                for l in range(LOTS):
                    pe.wait_ge(n_ready[l], g + 1)
                    lot_product(pe, ps[l][0], S1[:, l], S1[:, l]).then_inc(product_ready[l], 1)
                for l in range(LOTS):
                    pe.wait_ge(g_ready[l], g + 1)
                    lot_product(pe, ps[l][1], S2[:, l], H1[:, l]).then_inc(product_ready[l], 1)
                for l in range(LOTS):
                    pe.wait_ge(h_ready[l], g + 1)
                    lot_product(pe, ps[l][0], H1[:, l], H2[:, l]).then_inc(product_ready[l], 1)
                for s in range(SQUARINGS):
                    for l in range(LOTS):
                        if s == 0:
                            pe.wait_ge(e_ready[l], g + 1)
                        else:
                            pe.wait_ge(taken[l], g * TAKEN + 2 + s)
                        power = (S1, S2)[s % 2]
                        lot_product(pe, ps[l][(s + 1) % 2], power[:, l], power[:, l]).then_inc(product_ready[l], 1)

        @block.scalar
        def _(act):
            with act.Fori(0, GROUPS) as g:
                for l in range(LOTS):
                    act.wait_ge(product_ready[l], g * PRODUCTS + 1)
                    nc.scalar.copy(S2[:, l, :], ps[l][0][:, :]).then_inc(taken[l], 1)
                for l in range(LOTS):
                    act.wait_ge(product_ready[l], g * PRODUCTS + 2)
                    nc.scalar.mul(ZT[:, l, :], ps[l][1][:, :], z2).then_inc(taken[l], 1)
                for s in range(SQUARINGS - 1):
                    for l in range(LOTS):
                        act.wait_ge(product_ready[l], g * PRODUCTS + 4 + s)
                        nc.scalar.copy((S2, S1)[s % 2][:, l, :], ps[l][(s + 1) % 2][:, :]).then_inc(taken[l], 1)

        @block.vector
        def _(dve):
            dve.wait_ge(consts, 2)
            with dve.Fori(0, GROUPS) as g:
                for l in range(LOTS):
                    dve.wait_ge(m_loaded[l], 16 * LOT * g + 16 * LOT)
                    nc.vector.scalar_tensor_tensor(S1[:, l, :], M[:, l, :], 2.0 ** -SQUARINGS, shift[:, :],
                                                   ALU.mult, ALU.add).then_inc(n_ready[l], 1)
                for l in range(LOTS):
                    dve.wait_ge(n_ready[l], g + 1)
                    nc.vector.scalar_tensor_tensor(LO[:, l, :], S1[:, l, :], w1, last_term[:, :],
                                                   ALU.mult, ALU.add).then_inc(lo_done[l], 1)
                for l in range(LOTS):
                    dve.wait_ge(taken[l], g * TAKEN + 1)
                    nc.vector.scalar_tensor_tensor(H1[:, l, :], S1[:, l, :], z1 / z2, S2[:, l, :],
                                                   ALU.mult, ALU.add).then_inc(g_ready[l], 1)
                for l in range(LOTS):
                    dve.wait_ge(lo_done[l], g * 3 + 1)
                    nc.vector.scalar_tensor_tensor(LO[:, l, :], S2[:, l, :], w2, LO[:, l, :],
                                                   ALU.mult, ALU.add).then_inc(lo_done[l], 1)
                for l in range(LOTS):
                    dve.wait_ge(taken[l], g * TAKEN + 2)
                    nc.vector.scalar_tensor_tensor(H1[:, l, :], S1[:, l, :], u1, ZT[:, l, :],
                                                   ALU.mult, ALU.add).then_inc(h_step[l], 1)
                    nc.vector.scalar_tensor_tensor(H2[:, l, :], S2[:, l, :], v2, ZT[:, l, :],
                                                   ALU.mult, ALU.add)
                    dve.wait_ge(h_step[l], g + 1)
                    nc.vector.scalar_tensor_tensor(H1[:, l, :], S2[:, l, :], u2, H1[:, l, :],
                                                   ALU.mult, ALU.add).then_inc(h_ready[l], 1)
                for l in range(LOTS):
                    dve.wait_ge(lo_done[l], g * 3 + 2)
                    nc.vector.scalar_tensor_tensor(LO[:, l, :], ZT[:, l, :], w0, LO[:, l, :],
                                                   ALU.mult, ALU.add).then_inc(lo_done[l], 1)
                for l in range(LOTS):
                    dve.wait_ge(product_ready[l], g * PRODUCTS + 3)
                    dve.wait_ge(lo_done[l], g * 3 + 3)
                    nc.vector.scalar_tensor_tensor(S1[:, l, :], ps[l][0][:, :], MIDDLE, LO[:, l, :],
                                                   ALU.mult, ALU.add).then_inc(e_ready[l], 1)
                for l in range(LOTS):
                    dve.wait_ge(product_ready[l], g * PRODUCTS + PRODUCTS)
                    dve.wait_ge(x_loaded[l], 16 * LOT * g + 16 * LOT)
                    dve.wait_ge(stored[l], 16 * LOT * g + 1)
                    nc.vector.tensor_tensor(OUT[:, l, :], ps[l][SQUARINGS % 2][:, :], XR[:, l, :],
                                            ALU.add).then_inc(out_ready[l], 1)


def conv_layers(nc, x1, w_ring, bias_in, w_conv2, w_conv3, out):
    B = x1.shape[0]
    TILES = B // BB
    BUFS = 2
    PIX = N * N
    CONVS = 2
    x1_v = x1.rearrange("(t b) c h w -> t (b c) (h w)", b=BB)
    out_v = out.rearrange("(t b) c h w -> t (b c) (h w)", b=BB)

    with ExitStack() as ctx:
        def sb(name, shape):
            return ctx.enter_context(nc.sbuf_tensor(name, shape, F32))

        def sem(name):
            return ctx.enter_context(nc.semaphore(name))

        def sems(name, n=BUFS):
            return [sem(f"{name}{i}") for i in range(n)]

        mask = sb("net_mask", [P, P])
        pairs = sb("net_pairs", [P, P])
        eps = sb("net_eps", [P, 1])
        bias = sb("net_bias", [P, 1])
        ring_rows = sb("net_ring_rows", [P, C])
        taps_rows = sb("net_taps_rows", [P, CONVS, TAPS * TAPS * C])
        ring = sb("net_ring", [P, P])
        taps = sb("net_taps", [P, CONVS, TAPS * TAPS, P])
        X = sb("net_X", [P, BUFS, PIX])
        PAD = sb("net_PAD", [P, BUFS, PADN, PADN])
        Yt = sb("net_Y", [P, BUFS, PIX])
        bn = sb("net_bn", [P, BUFS, CHUNKS, 6])
        col = sb("net_col", [P, BUFS, 16])
        ps = [[ctx.enter_context(nc.psum_tensor(f"net_ps{i}{h}", [P, 2 * BANK], F32)) for h in range(2)]
              for i in range(BUFS)]

        w_loaded = sem("net_w_loaded")
        mask_step = sem("net_mask_step")
        consts = sem("net_consts")
        weights_ready = sem("net_weights_ready")
        loaded = sems("net_loaded")
        stored = sems("net_stored")
        bn_ready = sems("net_bn_ready")
        diff_ready = sems("net_diff")
        rstd_ready = sems("net_rstd")
        range_step = sems("net_range_step")
        minmax_ready = sems("net_minmax")
        summed = sems("net_summed")
        border_step = sems("net_border_step")
        mean_in = sems("net_mean_in")
        mean_out = sems("net_mean_out")
        var_in = sems("net_var_in")
        var_out = sems("net_var_out")
        std_ready = sems("net_std")
        norm_ready = sems("net_norm")
        inner_ready = sems("net_inner")
        padded = sems("net_padded")
        quarter_ready = sems("net_quarter")
        quarter_taken = sems("net_quarter_taken")
        leaky_ready = sems("net_leaky")
        scaled_ready = sems("net_scaled")
        block = ctx.enter_context(nc.Block())


        TURNS = TILES // BUFS
        QUARTERS = 4
        QROWS = N // QUARTERS
        PER_TURN = QUARTERS * (1 + CONVS)
        MEAN, VAR, DIFF, SPREAD, STD, RSTD, SHIFT, GMEAN, LOW, HIGH, RANGE, INV, LSHIFT = range(13)

        FIRST = [(0, 0, 0), (0, 1, 0), (1, 0, 0), (0, 2, 0), (1, 1, 0)]

        def turn(t):
            return [(0, 0, t), (1, 2, t - 1), (0, 1, t), (1, 0, t), (0, 2, t), (1, 1, t)]

        def cell(i, k):
            return col[:, i, k:k + 1]

        def run(engine, layer, prepare):
            def sequence(steps, after):
                for now, nxt in zip(steps, steps[1:] + [after]):
                    ahead = nxt if nxt is not None and nxt[0] != now[0] else None
                    layer(now, ahead)
                    if nxt is not None and ahead is None:
                        prepare(*nxt)

            prepare(*FIRST[0])
            sequence(FIRST, (0, 0, 1))
            if TURNS > 2:
                with engine.Fori(1, TURNS - 1) as t:
                    sequence(turn(t), (0, 0, t + 1))
            sequence(turn(TURNS - 1) + [(1, 2, TURNS - 1)], None)

        @block.gpsimd
        def _(pool):
            build_block_mask(pool, mask, mask_step, consts)
            pairs_v = pairs[:, :].rearrange("p (b c) -> p b c", c=2)
            pool.memset(pairs[:, :], 0.5).then_inc(mask_step, 1)
            pool.wait_ge(mask_step, 3)
            pool.affine_select(out=pairs_v, in_=pairs_v, compare_op=ALU.is_ge, fill=0.0, base=0,
                               pattern=[[-2, P // 2], [0, 2]], channel_multiplier=1).then_inc(mask_step, 1)
            pool.wait_ge(mask_step, 4)
            pool.affine_select(out=pairs_v, in_=pairs_v, compare_op=ALU.is_ge, fill=0.0, base=1,
                               pattern=[[2, P // 2], [0, 2]], channel_multiplier=-1).then_inc(consts, 1)
            pool.memset(eps[:, :], GN_EPS).then_inc(consts, 1)

            def border(i, j, t):
                pool.wait_ge(inner_ready[i], 3 * t + j + 1)
                pool.nop(nofuse=True)
                pool.tensor_copy(PAD[:, i, 1:N + 1, 0:1], PAD[:, i, 1:N + 1, N:N + 1])
                pool.tensor_copy(PAD[:, i, 1:N + 1, N + 1:N + 2],
                                 PAD[:, i, 1:N + 1, 1:2]).then_inc(border_step[i], 1)
                pool.wait_ge(border_step[i], CONVS * t + j)
                pool.nop(nofuse=True)
                pool.tensor_copy(PAD[:, i, 0:1, :], PAD[:, i, N:N + 1, :])
                pool.tensor_copy(PAD[:, i, N + 1:N + 2, :], PAD[:, i, 1:2, :]).then_inc(padded[i], 1)

            def prepare(i, j, t):
                if j > 0:
                    border(i, j, t)

            def layer(now, ahead):
                if ahead is not None:
                    prepare(*ahead)

            run(pool, layer, prepare)

        @block.sync
        def _(sp):
            sp.dma_start(ring_rows[:, :], w_ring).then_inc(w_loaded, 16)
            sp.dma_start(bias[:, :], bias_in).then_inc(w_loaded, 16)
            sp.dma_start(taps_rows[:, 0, :], w_conv2).then_inc(w_loaded, 16)
            sp.dma_start(taps_rows[:, 1, :], w_conv3).then_inc(w_loaded, 16)
            for i in range(BUFS):
                sp.dma_start(X[:, i, :], x1_v[i]).then_inc(loaded[i], 16)

            def replace(i, t, more):
                sp.wait_ge(quarter_taken[i], PER_TURN * t + PER_TURN)
                sp.dma_start(out_v[t * BUFS + i], X[:, i, :]).then_inc(stored[i], 16)
                sp.wait_ge(stored[i], 16 * t + 16)
                if more:
                    sp.dma_start(X[:, i, :], x1_v[(t + 1) * BUFS + i]).then_inc(loaded[i], 16)

            replace(0, 0, True)
            if TURNS > 2:
                with sp.Fori(1, TURNS - 1) as t:
                    replace(1, t - 1, True)
                    replace(0, t, True)
            replace(1, TURNS - 2, True)
            replace(0, TURNS - 1, False)
            replace(1, TURNS - 1, False)

        @block.tensor
        def _(pe):
            pe.wait_ge(weights_ready, 1)
            pe.wait_ge(consts, 3)

            def group_mean(i, j, t):
                pe.wait_ge(mean_in[i], 3 * t + j + 1)
                pe.matmul(ps[i][0][:, 0:1], pairs[:, :], cell(i, MEAN), start=True, stop=True).then_inc(mean_out[i], 1)

            def group_var(i, j, t):
                pe.wait_ge(var_in[i], 3 * t + j + 1)
                pe.matmul(ps[i][1][:, 0:1], pairs[:, :], cell(i, SPREAD), start=True, stop=True).then_inc(var_out[i], 1)

            def quarter(i, j, t, q):
                if q >= 2:
                    pe.wait_ge(quarter_taken[i], PER_TURN * t + QUARTERS * j + q - 1)
                for r in range(2):
                    row = q * QROWS + r * ROWS
                    o = ps[i][q % 2][:, r * BANK:(r + 1) * BANK]
                    if j == 0:
                        last = pe.matmul(o, ring[:, :], PAD[:, i, 1 + row:1 + row + ROWS, 1:1 + N],
                                         start=True, stop=True)
                        continue
                    for tap in range(TAPS * TAPS):
                        dy, dx = TAPS - 1 - tap // TAPS, TAPS - 1 - tap % TAPS
                        last = pe.matmul(o, taps[:, j - 1, tap, :],
                                         PAD[:, i, row + dy:row + dy + ROWS, dx:dx + N],
                                         start=(tap == 0), stop=(tap == TAPS * TAPS - 1))
                last.then_inc(quarter_ready[i], 1)

            def prepare(i, j, t):
                group_mean(i, j, t)
                group_var(i, j, t)

            def layer(now, ahead):
                i, j, t = now
                if j == 0:
                    pe.wait_ge(inner_ready[i], 3 * t + 1)
                else:
                    pe.wait_ge(padded[i], CONVS * t + j)
                quarter(i, j, t, 0)
                quarter(i, j, t, 1)
                if ahead is not None:
                    group_mean(*ahead)
                quarter(i, j, t, 2)
                if ahead is not None:
                    group_var(*ahead)
                quarter(i, j, t, 3)

            run(pe, layer, prepare)

        @block.scalar
        def _(act):
            act.wait_ge(consts, 3)
            act.wait_ge(w_loaded, 64)

            def normalise(i, j, t):
                act.wait_ge(var_out[i], 3 * t + j + 1)
                nc.scalar.activation(cell(i, STD), ps[i][1][:, 0:1], ACT.Sqrt, bias=eps[:, 0:1],
                                     scale=1.0).then_inc(std_ready[i], 1)
                act.wait_ge(norm_ready[i], 3 * t + j + 1)
                nc.scalar.activation(PAD[:, i, 1:N + 1, 1:N + 1], X[:, i, :].rearrange("p (h w) -> p h w", w=N),
                                     ACT.Identity, bias=cell(i, SHIFT), scale=cell(i, RSTD)).then_inc(inner_ready[i], 1)

            def add_bias(i, t, q):
                act.wait_ge(quarter_ready[i], PER_TURN * t + q + 1)
                nc.scalar.activation(Yt[:, i, q * 2 * BANK:(q + 1) * 2 * BANK], ps[i][q % 2][:, :], ACT.Identity,
                                     bias=bias[:, 0:1], scale=1.0).then_inc(quarter_taken[i], 1)

            def layer(now, ahead):
                i, j, t = now
                if j == 0:
                    for q in range(QUARTERS):
                        add_bias(i, t, q)
                if ahead is not None:
                    normalise(*ahead)
                if j == 0:
                    act.wait_ge(minmax_ready[i], t + 1)
                    nc.scalar.activation(Yt[:, i, :], Yt[:, i, :], ACT.Identity, bias=cell(i, LSHIFT),
                                         scale=cell(i, INV)).then_inc(scaled_ready[i], 1)

            run(act, layer, normalise)

        @block.vector
        def _(dve):
            dve.wait_ge(w_loaded, 64)
            dve.wait_ge(consts, 3)
            mask_v = mask[:, :].rearrange("p (b c) -> p b c", c=C)
            nc.vector.tensor_tensor(ring[:, :].rearrange("p (b c) -> p b c", c=C), mask_v,
                                    ring_rows[:, :].unsqueeze(1).to_broadcast([P, BB, C]), ALU.mult)
            for v in range(CONVS):
                for tap in range(TAPS * TAPS):
                    rows = taps_rows[:, v, tap * C:(tap + 1) * C]
                    last = nc.vector.tensor_tensor(taps[:, v, tap, :].rearrange("p (b c) -> p b c", c=C), mask_v,
                                                   rows.unsqueeze(1).to_broadcast([P, BB, C]), ALU.mult)
            last.then_inc(weights_ready, 1)

            def statistics(i, j, t):
                if j == 0:
                    dve.wait_ge(loaded[i], 16 * t + 16)
                elif j == 1:
                    dve.wait_ge(summed[i], t + 1)
                else:
                    dve.wait_ge(quarter_taken[i], PER_TURN * t + QUARTERS * j)
                for k in range(CHUNKS):
                    last = nc.vector.bn_stats(bn[:, i, k, :], X[:, i, k * BANK:(k + 1) * BANK])
                last.then_inc(bn_ready[i], 1)
                dve.wait_ge(bn_ready[i], 3 * t + j + 1)
                dve.nop(nofuse=True)
                nc.vector.bn_aggr(col[:, i, MEAN:VAR + 1], bn[:, i, :, :]).then_inc(mean_in[i], 1)

            def spread_about_group(i, j, t):
                dve.wait_ge(mean_out[i], 3 * t + j + 1)
                nc.vector.tensor_copy(cell(i, GMEAN), ps[i][0][:, 0:1])
                nc.vector.tensor_tensor(cell(i, DIFF), cell(i, MEAN), ps[i][0][:, 0:1],
                                        ALU.subtract).then_inc(diff_ready[i], 1)
                dve.wait_ge(diff_ready[i], 3 * t + j + 1)
                nc.vector.scalar_tensor_tensor(cell(i, SPREAD), cell(i, DIFF), cell(i, DIFF), cell(i, VAR),
                                               ALU.mult, ALU.add).then_inc(var_in[i], 1)

            def scale_and_shift(i, j, t):
                dve.wait_ge(std_ready[i], 3 * t + j + 1)
                nc.vector.reciprocal(cell(i, RSTD), cell(i, STD)).then_inc(rstd_ready[i], 1)
                dve.wait_ge(rstd_ready[i], 3 * t + j + 1)
                nc.vector.scalar_tensor_tensor(cell(i, SHIFT), cell(i, GMEAN), -1.0, cell(i, RSTD),
                                               ALU.mult, ALU.mult).then_inc(norm_ready[i], 1)

            def take(i, j, t, q):
                span = slice(q * 2 * BANK, (q + 1) * 2 * BANK)
                if j == 0:
                    dve.wait_ge(quarter_taken[i], PER_TURN * t + q + 1)
                    nc.vector.scalar_tensor_tensor(Yt[:, i, span], Yt[:, i, span], SLOPE, Yt[:, i, span],
                                                   ALU.mult, ALU.max).then_inc(leaky_ready[i], 1)
                else:
                    dve.wait_ge(quarter_ready[i], PER_TURN * t + QUARTERS * j + q + 1)
                    nc.vector.tensor_tensor(X[:, i, span], ps[i][q % 2][:, :], X[:, i, span],
                                            ALU.add).then_inc(quarter_taken[i], 1)

            def min_max(i, t):
                dve.wait_ge(leaky_ready[i], QUARTERS * t + QUARTERS)
                nc.vector.tensor_reduce(cell(i, LOW), Yt[:, i, :], AX.X, ALU.min)
                nc.vector.tensor_reduce(cell(i, HIGH), Yt[:, i, :], AX.X, ALU.max).then_inc(range_step[i], 1)
                dve.wait_ge(range_step[i], 3 * t + 1)
                nc.vector.tensor_scalar(cell(i, RANGE), cell(i, HIGH), cell(i, LOW), MINMAX_EPS,
                                        ALU.subtract, ALU.add).then_inc(range_step[i], 1)
                dve.wait_ge(range_step[i], 3 * t + 2)
                nc.vector.reciprocal(cell(i, INV), cell(i, RANGE)).then_inc(range_step[i], 1)
                dve.wait_ge(range_step[i], 3 * t + 3)
                nc.vector.scalar_tensor_tensor(cell(i, LSHIFT), cell(i, LOW), -1.0, cell(i, INV),
                                               ALU.mult, ALU.mult).then_inc(minmax_ready[i], 1)

            def prepare(i, j, t):
                statistics(i, j, t)
                spread_about_group(i, j, t)
                scale_and_shift(i, j, t)

            def layer(now, ahead):
                i, j, t = now
                take(i, j, t, 0)
                if ahead is not None:
                    statistics(*ahead)
                take(i, j, t, 1)
                if ahead is not None:
                    spread_about_group(*ahead)
                take(i, j, t, 2)
                if ahead is not None:
                    scale_and_shift(*ahead)
                take(i, j, t, 3)
                if j == 0:
                    min_max(i, t)
                    dve.wait_ge(scaled_ready[i], t + 1)
                    nc.vector.tensor_tensor(X[:, i, :], X[:, i, :], Yt[:, i, :], ALU.add).then_inc(summed[i], 1)

            run(dve, layer, prepare)


def kernel(**inputs):
    import numpy as _np
    import concourse.bacc as _bacc
    from concourse import mybir as _mybir
    from concourse.bass_utils import run_bass_kernel_spmd as _run

    nc = _bacc.Bacc("TRN2", target_bir_lowering=False, num_devices=1)
    x = _np.ascontiguousarray(inputs["x"])
    c = x.shape[1]
    ring = _np.ascontiguousarray(inputs["L1_conv_w"])
    arrays = {
        "x": x,
        "w_mix": _np.tile(inputs["L0_conv_weights"], (128 // c, 1)),
        "w_ring": _np.tile(_np.stack([_np.roll(ring, o) for o in range(c)], axis=1), (128 // c, 1)),
        "bias": _np.tile(_np.ascontiguousarray(inputs["L1_conv_b"]), (128, 1)),
    }
    for name in ("L2_conv_weight", "L3_conv_weight"):
        w = _np.asarray(inputs[name])
        w = _np.transpose(w, (1, 2, 3, 0)).reshape(c, -1)
        arrays[name] = _np.ascontiguousarray(_np.tile(w, (128 // c, 1)))
    args = []
    for name, a in arrays.items():
        args.append(nc.dram_tensor(f"in_{name}", a.shape, _mybir.dt.from_np(a.dtype), kind="ExternalInput").ap())
    args.append(nc.dram_tensor("out_0", x.shape, _mybir.dt.float32, kind="ExternalOutput").ap())
    build(nc, *args)
    r = _run(nc, [{f"in_{k}": v for k, v in arrays.items()}], core_ids=[0])
    return r.results[0]["out_0"]
```
